# Optimizing a Trainium2 kernel written in Bass

```python
import numpy as np
import jax
import jax.numpy as jnp

def _softmax(x, axis=-1):
    return jax.nn.softmax(x, axis=axis)

def _gelu(x):
    return jax.nn.gelu(x, approximate=True)

def _silu(x):
    return jax.nn.silu(x)

def _sigmoid(x):
    return jax.nn.sigmoid(x)

def _layernorm(x, axis=-1, eps=1e-05):
    m = jnp.mean(x, axis=axis, keepdims=True)
    v = jnp.var(x, axis=axis, keepdims=True)
    return (x - m) / jnp.sqrt(v + eps)

def _scatter_add(tgt, idx, src, axis=0):
    return tgt.at[idx].add(src)

def _segment_sum(src, seg, n):
    return jax.ops.segment_sum(src, seg, n)
kernel_name = 'mk_adj_preln_d1_adj_r2_4ea8b2'

def setup_inputs(seed: int=0):
    np.random.seed(seed)
    _w = jnp.asarray

    def _rec_inputs():
        import jax
        import jax.numpy as jnp
        _gk = jax.random.key(seed)
        x = -0.0002928 + 1 * jax.random.normal(jax.random.fold_in(_gk, 1), (8192, 128), jnp.float32)
        _w = (1.0 + jnp.arange(8192, dtype=jnp.float32)) ** (-0.5)
        _w = _w / _w.mean()
        _pij = jnp.clip(0.000488281 * _w[:, None] * _w[None, :], 0.0, 1.0)
        _a = jax.random.uniform(jax.random.fold_in(_gk, 2), (8192, 8192)) < _pij
        _a = jnp.logical_or(_a, jnp.eye(8192, dtype=bool))
        _af = _a.astype(jnp.float32)
        _af = _af * jax.random.uniform(jax.random.fold_in(_gk, 3), (8192, 8192), jnp.float32, 0.05, 1)
        adj = _af
        return (x, adj)
    x, adj = _rec_inputs()

    def _L0_gnn_setup():
        import jax, jax.numpy as jnp
        import numpy as np
        N, D_IN, D_OUT = (8192, 128, 128)
        key = jax.random.key(seed)
        k1, k2, k3, k4 = jax.random.split(key, 4)
        x = jax.random.normal(k1, (N, D_IN), dtype=jnp.float32)
        adj = jax.random.uniform(k2, (N, N), dtype=jnp.float32)
        W = jax.random.normal(k3, (D_IN, D_OUT), dtype=jnp.float32) / np.sqrt(D_IN)
        b = jax.random.normal(k4, (D_OUT,), dtype=jnp.float32) * 0.01
        return {'x': x, 'adj': adj, 'W': W, 'b': b}
    _L0_gnn_all = _L0_gnn_setup()
    _L0_gnn_in = {k: v for k, v in _L0_gnn_all.items() if k in ('W', 'b')}
    del _L0_gnn_all
    return {'x': x, 'adj': adj, 'L0_gnn_W': _L0_gnn_in['W'], 'L0_gnn_b': _L0_gnn_in['b']}

def reference(x, adj, L0_gnn_W, L0_gnn_b):
    import jax
    import jax.numpy as jnp

    def _L0_gnn_ref(x, adj, W, b):
        import jax, jax.numpy as jnp
        import numpy as np
        N, D_IN, D_OUT = (8192, 128, 128)
        support = jnp.matmul(x, W)
        out = jnp.matmul(adj, support) + b
        return jax.nn.relu(out)
    h = jnp.maximum(_layernorm(x, axis=-1), 0.0)
    x = x + _L0_gnn_ref(h, adj, L0_gnn_W, L0_gnn_b)
    return x

_drawn_inputs = setup_inputs


def setup_inputs(seed=0):
    import zlib

    import numpy as np

    out = dict(_drawn_inputs(seed))
    spreads = {}
    factors = {'L0_gnn_b': 8.0}
    for name, (base, spread) in spreads.items():
        noise = np.random.default_rng([zlib.crc32(name.encode()), seed]).standard_normal(out[name].shape)
        drawn = base * np.exp(spread * noise) if base else spread * noise
        out[name] = jnp.asarray(drawn.astype(out[name].dtype))
    for name, factor in factors.items():
        out[name] = (out[name] * factor).astype(out[name].dtype)
    return out
```

```python
from contextlib import ExitStack

import concourse.bass as bass
from concourse import mybir

P = 128
BANK = 512
N = 8192
TILES = N // P
COL_BLOCKS = N // BANK
PSUM_BANKS = 8
UNROLL = BANK // P
ROUNDS = TILES // UNROLL
WIDTHS = [6, 6, 4]
FIRST_BLOCK = [0, 6, 12]
ADJ_SLOTS = UNROLL
SPLIT_SLOTS = 2
WEIGHT_SLOTS = UNROLL
CENTER_BANK, SUPPORT_BANK = 6, 7
EPS = 1e-5

ALU = mybir.AluOpType
ACT = mybir.ActivationFunctionType
F32 = mybir.dt.float32
F32R = mybir.dt.float32r


def gnn_layer(nc, x_blocks, adj_groups, W, b, out_blocks):
    assert sum(WIDTHS) == COL_BLOCKS and ADJ_SLOTS == WEIGHT_SLOTS == UNROLL
    with ExitStack() as ctx:
        def sb(name, shape, dt=F32):
            return ctx.enter_context(nc.sbuf_tensor(name, shape, dt))

        def sem(name):
            return ctx.enter_context(nc.semaphore(name))

        widest = max(WIDTHS) * BANK
        xT = sb("xT", [P, COL_BLOCKS, BANK])
        support = sb("support", [P, TILES, P])
        adj_tile = sb("adj_tile", [P, ADJ_SLOTS, widest])
        adj_high = sb("adj_high", [P, SPLIT_SLOTS, widest], F32R)
        adj_low = sb("adj_low", [P, SPLIT_SLOTS, widest], F32R)
        sup_full = sb("sup_full", [P, WEIGHT_SLOTS, P])
        sup_high = sb("sup_high", [P, WEIGHT_SLOTS, P], F32R)
        sup_low = sb("sup_low", [P, WEIGHT_SLOTS, P], F32R)
        W_sb = sb("W_sb", [P, P])
        bias = sb("bias", [P, 1])
        centering = sb("centering", [P, P])
        mean_col = sb("mean_col", [P, 1])
        minus_half = sb("minus_half", [P, UNROLL])
        squares = sb("squares", [P, BANK])
        rectified = sb("rectified", [P, BANK])
        var_eps = sb("var_eps", [P, UNROLL])
        rstd = sb("rstd", [P, UNROLL])
        relu_out = sb("relu_out", [P, 2, BANK])
        banks = ctx.enter_context(nc.psum_tensor("banks", [P, PSUM_BANKS, BANK], F32))
        centered_ps = banks[:, CENTER_BANK, :]
        var_ps = banks[:, CENTER_BANK, 0:UNROLL]
        support_ps = banks[:, SUPPORT_BANK, :]

        adj_landed = [sem(f"adj_landed{s}") for s in range(ADJ_SLOTS)]
        x_landed = sem("x_landed")
        params_landed = sem("params_landed")
        centering_zeroed = sem("centering_zeroed")
        constants_ready = sem("constants_ready")
        high_ready = sem("high_ready")
        low_ready = sem("low_ready")
        sup_high_ready = sem("sup_high_ready")
        weights_ready = sem("weights_ready")
        products_done = sem("products_done")
        centered = sem("centered")
        squared = sem("squared")
        rectified_ready = sem("rectified_ready")
        projected = sem("projected")
        var_ready = sem("var_ready")
        rstd_ready = sem("rstd_ready")
        support_ready = sem("support_ready")
        bank_drained = sem("bank_drained")
        output_ready = sem("output_ready")
        groups_stored = sem("groups_stored")
        banks_stored = sem("banks_stored")
        block = ctx.enter_context(nc.Block())

        def in_all_groups(eng, round_steps):
            round_steps(0, 0, True, True)
            with eng.Fori(1, ROUNDS - 2) as k:
                round_steps(0, k, True, True)
            round_steps(0, ROUNDS - 2, True, False)
            round_steps(0, ROUNDS - 1, False, False)
            for g in range(1, len(WIDTHS)):
                round_steps(g, 0, False, False)
                with eng.Fori(1, ROUNDS - 1) as k:
                    round_steps(g, k, False, False)
                round_steps(g, ROUNDS - 1, False, False)

        def step_of(g, k, r):
            return k * UNROLL + (g * TILES + r)

        def landed_count(g, k):
            return k * 16 + 16 * (g * ROUNDS + 1)

        @block.sync
        def _(sp):
            sp.dma_start(xT[:, 0, :], x_blocks[0]).then_inc(x_landed, 16)
            sp.dma_start(W_sb[:, :], W).then_inc(params_landed, 16)
            sp.dma_start(bias[:, :], b).then_inc(params_landed, 16)

            def load_x(n):
                sp.wait_ge(x_landed, n * 16)
                sp.dma_start(xT[:, bass.ds(n, 1), :], x_blocks[bass.ds(n, 1)].rearrange("o p c -> p o c"))\
                  .then_inc(x_landed, 16)

            def loads(g, k, stage_b, stage_a):
                width = WIDTHS[g] * BANK
                first = g == 0 and isinstance(k, int) and k == 0
                if first:
                    load_x(1)
                for r in range(UNROLL):
                    if r == 2 and stage_a:
                        load_x(k + 2)
                    if not first:
                        sp.wait_ge(low_ready, step_of(g, k, r) - (ADJ_SLOTS - 1))
                    sp.dma_start(adj_tile[:, r:r + 1, 0:width],
                                 adj_groups[g][bass.ds(k * UNROLL + r, 1)].rearrange("o p c -> p o c"))\
                      .then_inc(adj_landed[r], 16)

            in_all_groups(sp, loads)
            for n in range(FIRST_BLOCK[-1], COL_BLOCKS):
                sp.wait_ge(output_ready, n + 1)
                sp.dma_start(out_blocks[n], xT[:, n, :]).then_inc(banks_stored, 16)
            sp.wait_ge(banks_stored, 16 * WIDTHS[-1])

        @block.gpsimd
        def _(pool):
            nc.gpsimd.memset(centering[:, :], -1.0 / P).then_inc(centering_zeroed, 1)
            nc.gpsimd.memset(mean_col[:, :], 1.0 / P).then_inc(constants_ready, 1)
            nc.gpsimd.memset(minus_half[:, :], -0.5).then_inc(constants_ready, 1)
            pool.wait_ge(centering_zeroed, 1)
            nc.gpsimd.affine_select(out=centering[:, :], in_=centering[:, :], compare_op=ALU.not_equal,
                                    fill=1.0 - 1.0 / P, base=0, pattern=[[-1, P]],
                                    channel_multiplier=1).then_inc(constants_ready, 1)
            pool.wait_ge(constants_ready, 3)

            def inverse_deviation(n):
                pool.wait_ge(var_ready, n + 1)
                if not (isinstance(n, int) and n == 0):
                    pool.wait_ge(support_ready, n)
                nc.gpsimd.tensor_tensor(rstd[:, :], var_eps[:, :], minus_half[:, :], ALU.pow)\
                    .then_inc(rstd_ready, 1)

            def weights(g, k, stage_b, stage_a):
                start = isinstance(k, int) and k == 0
                if g == 0:
                    pool.wait_ge(support_ready, k + 1)
                for r in range(UNROLL):
                    t = step_of(g, k, r)
                    if stage_b and r == 3:
                        inverse_deviation(k + 1)
                    if not (g == 0 and start):
                        pool.wait_ge(products_done, t - (WEIGHT_SLOTS - 1))
                    tile = support[:, bass.ds(k * UNROLL + r, 1), :]
                    nc.gpsimd.tensor_copy(sup_full[:, r:r + 1, :], tile).then_inc(sup_high_ready, 1)
                    nc.gpsimd.tensor_copy(sup_high[:, r:r + 1, :], tile).then_inc(sup_high_ready, 1)
                    pool.wait_ge(sup_high_ready, t * 2 + 2)
                    nc.gpsimd.tensor_tensor(sup_low[:, r, :], sup_full[:, r, :],
                                            sup_high[:, r, :].bitcast(F32), ALU.subtract)\
                        .then_inc(weights_ready, 1)
                if g > 0 and start:
                    first, last = FIRST_BLOCK[g - 1], FIRST_BLOCK[g]
                    pool.wait_ge(output_ready, last)
                    pool.dma_start(out_blocks[first:last].rearrange("n p c -> p n c"),
                                   xT[:, first:last, :]).then_inc(groups_stored, 16)

            inverse_deviation(0)
            in_all_groups(pool, weights)
            pool.wait_ge(groups_stored, 16 * (len(WIDTHS) - 1))

        @block.scalar
        def _(act):
            def square(n):
                act.wait_ge(rectified_ready, n + 1)
                nc.scalar.activation(squares[:, :], centered_ps, ACT.Square).then_inc(squared, 1)

            def drain(g):
                act.wait_ge(products_done, (g + 1) * TILES)
                for n in range(FIRST_BLOCK[g], FIRST_BLOCK[g] + WIDTHS[g]):
                    if n >= 2:
                        act.wait_ge(output_ready, n - 1)
                    nc.scalar.activation(relu_out[:, n % 2, :], banks[:, n % PSUM_BANKS, :], ACT.Relu,
                                         bias=bias[:, 0:1]).then_inc(bank_drained, 1)

            def round_high(g, k, stage_b, stage_a):
                start = isinstance(k, int) and k == 0
                width = WIDTHS[g] * BANK
                for r in range(UNROLL):
                    t = step_of(g, k, r)
                    act.wait_ge(adj_landed[r], landed_count(g, k))
                    if not (g == 0 and start and r < SPLIT_SLOTS):
                        act.wait_ge(products_done, t - (SPLIT_SLOTS - 1))
                    nc.scalar.activation(adj_high[:, r % SPLIT_SLOTS, 0:width], adj_tile[:, r, 0:width],
                                         ACT.Copy).then_inc(high_ready, 1)
                    if stage_a and r == 3:
                        square(k + 2)
                    if g > 0 and start and r == 0:
                        drain(g - 1)

            square(0)
            act.wait_ge(params_landed, 32)
            square(1)
            in_all_groups(act, round_high)
            drain(len(WIDTHS) - 1)

        @block.vector
        def _(dve):
            def rectify(n):
                dve.wait_ge(centered, n + 1)
                nc.vector.tensor_scalar(rectified[:, :], centered_ps, 0.0, None, ALU.max)\
                    .then_inc(rectified_ready, 1)

            def variance(n):
                dve.wait_ge(projected, n + 1)
                nc.vector.tensor_scalar(var_eps[:, :], var_ps, EPS, None, ALU.add).then_inc(var_ready, 1)

            def scale_support(n):
                dve.wait_ge(rstd_ready, n + 1)
                nc.vector.tensor_tensor(support[:, bass.ds(n * UNROLL, UNROLL), :],
                                        support_ps.rearrange("p (t d) -> p t d", d=P),
                                        rstd[:, :].rearrange("p (t o) -> p t o", o=1)
                                        .to_broadcast([P, UNROLL, P]), ALU.mult)\
                    .then_inc(support_ready, 1)

            def add_x(g):
                for n in range(FIRST_BLOCK[g], FIRST_BLOCK[g] + WIDTHS[g]):
                    dve.wait_ge(bank_drained, n + 1)
                    nc.vector.tensor_tensor(xT[:, n, :], xT[:, n, :], relu_out[:, n % 2, :], ALU.add)\
                        .then_inc(output_ready, 1)

            def round_low(g, k, stage_b, stage_a):
                start = isinstance(k, int) and k == 0
                width = WIDTHS[g] * BANK
                for r in range(UNROLL):
                    dve.wait_ge(high_ready, step_of(g, k, r) + 1)
                    nc.vector.tensor_tensor(adj_low[:, r % SPLIT_SLOTS, 0:width], adj_tile[:, r, 0:width],
                                            adj_high[:, r % SPLIT_SLOTS, 0:width].bitcast(F32),
                                            ALU.subtract).then_inc(low_ready, 1)
                    if stage_b and r == 1:
                        variance(k + 1)
                    if stage_b and r == 2:
                        scale_support(k + 1)
                    if stage_a and r == 2:
                        rectify(k + 2)
                    if g > 0 and start and r == 0:
                        add_x(g - 1)

            rectify(0)
            variance(0)
            scale_support(0)
            rectify(1)
            in_all_groups(dve, round_low)
            add_x(len(WIDTHS) - 1)

        @block.tensor
        def _(pe):
            def center(n):
                pe.wait_ge(x_landed, n * 16 + 16)
                if not (isinstance(n, int) and n == 0):
                    pe.wait_ge(var_ready, n)
                nc.tensor.matmul(banks[:, CENTER_BANK:CENTER_BANK + 1, :], centering[:, :],
                                 xT[:, bass.ds(n, 1), :], start=True, stop=True).then_inc(centered, 1)

            def project(n):
                pe.wait_ge(squared, n + 1)
                if not (isinstance(n, int) and n == 0):
                    pe.wait_ge(support_ready, n)
                for i in range(UNROLL):
                    nc.tensor.matmul(var_ps[:, i:i + 1], squares[:, i * P:(i + 1) * P], mean_col[:, :],
                                     start=True, stop=True)
                for i in range(UNROLL):
                    last = nc.tensor.matmul(support_ps[:, i * P:(i + 1) * P],
                                            rectified[:, i * P:(i + 1) * P], W_sb[:, :],
                                            start=True, stop=True)
                last.then_inc(projected, 1)

            def round_products(g, k, stage_b, stage_a):
                start, end = (isinstance(k, int) and k == edge for edge in (0, ROUNDS - 1))
                for r in range(UNROLL):
                    t = step_of(g, k, r)
                    opens, closes = start and r == 0, end and r == UNROLL - 1
                    if stage_a and r == 2:
                        center(k + 2)
                    pe.wait_ge(weights_ready, t + 1)
                    pe.wait_ge(high_ready, t + 1)
                    parts = [(sup_high, adj_high), (sup_low, adj_high), (sup_high, adj_low)]
                    for i, (sup, adj) in enumerate(parts):
                        if i == 2:
                            pe.wait_ge(low_ready, t + 1)
                        for c in range(WIDTHS[g]):
                            n = FIRST_BLOCK[g] + c
                            if opens and i == 0 and n >= PSUM_BANKS:
                                pe.wait_ge(bank_drained, n - PSUM_BANKS + 1)
                            last = nc.tensor.matmul(banks[:, n % PSUM_BANKS, :], sup[:, r, :],
                                                    adj[:, r % SPLIT_SLOTS, c * BANK:(c + 1) * BANK],
                                                    start=opens and i == 0, stop=closes and i == 2)
                    last.then_inc(products_done, 1)
                if stage_a:
                    project(k + 2)

            pe.wait_ge(constants_ready, 3)
            center(0)
            pe.wait_ge(params_landed, 32)
            project(0)
            center(1)
            project(1)
            in_all_groups(pe, round_products)


def kernel(x, adj, L0_gnn_W, L0_gnn_b):
    import numpy as np
    import concourse.bacc as bacc
    from concourse.bass_utils import run_bass_kernel_spmd

    nc = bacc.Bacc("TRN2", target_bir_lowering=False, num_devices=1)
    x, adj = np.asarray(x), np.asarray(adj)
    arrays = {
        "x_blocks": np.ascontiguousarray(x.T.reshape(P, COL_BLOCKS, BANK).transpose(1, 0, 2)),
        "W": np.ascontiguousarray(L0_gnn_W),
        "b": np.ascontiguousarray(L0_gnn_b).reshape(P, 1),
    }
    for g, (first, width) in enumerate(zip(FIRST_BLOCK, WIDTHS)):
        rows = adj[first * BANK:(first + width) * BANK]
        arrays[f"adj{g}"] = np.ascontiguousarray(rows.T).reshape(TILES, P, width * BANK)
    ap = {name: nc.dram_tensor(name, a.shape, F32, kind="ExternalInput").ap() for name, a in arrays.items()}
    out = nc.dram_tensor("out_blocks", (COL_BLOCKS, P, BANK), F32, kind="ExternalOutput").ap()
    gnn_layer(nc, ap["x_blocks"], [ap[f"adj{g}"] for g in range(len(WIDTHS))], ap["W"], ap["b"], out)
    result = run_bass_kernel_spmd(nc, [arrays], core_ids=[0]).results[0]["out_blocks"]
    return np.ascontiguousarray(result.transpose(0, 2, 1)).reshape(N, P)
```

```python
from contextlib import ExitStack

import concourse.bass as bass
from concourse import mybir

P = 128
BANK = 512
N = 8192
TILES = N // P
COL_BLOCKS = N // BANK
PSUM_BANKS = 8
UNROLL = BANK // P
ROUNDS = TILES // UNROLL
WIDTHS = [6, 6, 4]
FIRST_BLOCK = [0, 6, 12]
ADJ_SLOTS = UNROLL
SPLIT_SLOTS = 2
WEIGHT_SLOTS = UNROLL
DRAINED = [[4, 2, 0, 0], [2, 2, 2, 0]]
STORED_LATE = range(3, FIRST_BLOCK[-1])
CENTER_BANK, SUPPORT_BANK = 6, 7
EPS = 1e-5

ALU = mybir.AluOpType
ACT = mybir.ActivationFunctionType
F32 = mybir.dt.float32
F32R = mybir.dt.float32r


def gnn_layer(nc, x_blocks, adj_groups, W, b, out_blocks):
    assert sum(WIDTHS) == COL_BLOCKS and ADJ_SLOTS == WEIGHT_SLOTS == UNROLL
    with ExitStack() as ctx:
        def sb(name, shape, dt=F32):
            return ctx.enter_context(nc.sbuf_tensor(name, shape, dt))

        def sem(name):
            return ctx.enter_context(nc.semaphore(name))

        widest = max(WIDTHS) * BANK
        xT = sb("xT", [P, COL_BLOCKS, BANK])
        support = sb("support", [P, TILES, P])
        adj_tile = sb("adj_tile", [P, ADJ_SLOTS, widest])
        adj_high = sb("adj_high", [P, SPLIT_SLOTS, widest], F32R)
        adj_low = sb("adj_low", [P, SPLIT_SLOTS, widest], F32R)
        sup_full = sb("sup_full", [P, WEIGHT_SLOTS, P])
        sup_high = sb("sup_high", [P, WEIGHT_SLOTS, P], F32R)
        sup_low = sb("sup_low", [P, WEIGHT_SLOTS, P], F32R)
        W_sb = sb("W_sb", [P, P])
        bias = sb("bias", [P, 1])
        centering = sb("centering", [P, P])
        mean_col = sb("mean_col", [P, 1])
        minus_half = sb("minus_half", [P, UNROLL])
        squares = sb("squares", [P, BANK])
        rectified = sb("rectified", [P, BANK])
        var_eps = sb("var_eps", [P, UNROLL])
        rstd = sb("rstd", [P, UNROLL])
        relu_out = sb("relu_out", [P, 2, BANK])
        banks = ctx.enter_context(nc.psum_tensor("banks", [P, PSUM_BANKS, BANK], F32))
        centered_ps = banks[:, CENTER_BANK, :]
        var_ps = banks[:, CENTER_BANK, 0:UNROLL]
        support_ps = banks[:, SUPPORT_BANK, :]

        adj_landed = [sem(f"adj_landed{s}") for s in range(ADJ_SLOTS)]
        piece_landed = [sem(f"piece_landed{c}") for c in range(WIDTHS[-1])]
        piece_high = sem("piece_high")
        piece_low = sem("piece_low")
        piece_products = sem("piece_products")
        x_landed = sem("x_landed")
        params_landed = sem("params_landed")
        centering_zeroed = sem("centering_zeroed")
        constants_ready = sem("constants_ready")
        high_ready = sem("high_ready")
        low_ready = sem("low_ready")
        sup_high_ready = sem("sup_high_ready")
        weights_ready = sem("weights_ready")
        products_done = sem("products_done")
        centered = sem("centered")
        squared = sem("squared")
        rectified_ready = sem("rectified_ready")
        projected = sem("projected")
        var_ready = sem("var_ready")
        rstd_ready = sem("rstd_ready")
        support_ready = sem("support_ready")
        bank_drained = sem("bank_drained")
        output_ready = sem("output_ready")
        early_stored = sem("early_stored")
        late_stored = sem("late_stored")
        banks_stored = sem("banks_stored")
        block = ctx.enter_context(nc.Block())

        def in_all_groups(eng, round_steps):
            round_steps(0, 0, True, True)
            with eng.Fori(1, ROUNDS - 2) as k:
                round_steps(0, k, True, True)
            round_steps(0, ROUNDS - 2, True, False)
            round_steps(0, ROUNDS - 1, False, False)
            for g in range(1, len(WIDTHS)):
                round_steps(g, 0, False, False)
                with eng.Fori(1, ROUNDS - 1) as k:
                    round_steps(g, k, False, False)
                round_steps(g, ROUNDS - 1, False, False)

        def step_of(g, k, r):
            return k * UNROLL + (g * TILES + r)

        def landed_count(g, k):
            return k * 16 + 16 * (g * ROUNDS + 1)

        def is_last(g, k, r):
            return g == len(WIDTHS) - 1 and isinstance(k, int) and k == ROUNDS - 1 and r == UNROLL - 1

        def drained_after(g, k, r):
            if g == 0 or not isinstance(k, int) or k > 0:
                return range(0)
            counts = DRAINED[g - 1]
            assert sum(counts) == WIDTHS[g - 1]
            first = FIRST_BLOCK[g - 1] + sum(counts[:r])
            return range(first, first + counts[r])

        @block.sync
        def _(sp):
            sp.dma_start(xT[:, 0, :], x_blocks[0]).then_inc(x_landed, 16)
            sp.dma_start(W_sb[:, :], W).then_inc(params_landed, 16)
            sp.dma_start(bias[:, :], b).then_inc(params_landed, 16)

            def load_x(n):
                sp.wait_ge(x_landed, n * 16)
                sp.dma_start(xT[:, bass.ds(n, 1), :], x_blocks[bass.ds(n, 1)].rearrange("o p c -> p o c"))\
                  .then_inc(x_landed, 16)

            def loads(g, k, stage_b, stage_a):
                width = WIDTHS[g] * BANK
                first = g == 0 and isinstance(k, int) and k == 0
                for r in range(UNROLL):
                    if first and r == 1:
                        load_x(1)
                    if r == 2 and stage_a:
                        load_x(k + 2)
                    if not first:
                        sp.wait_ge(low_ready, step_of(g, k, r) - (ADJ_SLOTS - 1))
                    if is_last(g, k, r):
                        for c in range(WIDTHS[g]):
                            cols = slice(c * BANK, (c + 1) * BANK)
                            sp.dma_start(adj_tile[:, r, cols], adj_groups[g][TILES - 1][:, cols])\
                              .then_inc(piece_landed[c], 16)
                        continue
                    sp.dma_start(adj_tile[:, r:r + 1, 0:width],
                                 adj_groups[g][bass.ds(k * UNROLL + r, 1)].rearrange("o p c -> p o c"))\
                      .then_inc(adj_landed[r], 16)

            in_all_groups(sp, loads)
            sp.wait_ge(output_ready, STORED_LATE[-1] + 1)
            late = slice(STORED_LATE[0], STORED_LATE[-1] + 1)
            sp.dma_start(out_blocks[late].rearrange("n p c -> p n c"), xT[:, late, :])\
              .then_inc(late_stored, 16)
            for n in range(FIRST_BLOCK[-1], COL_BLOCKS):
                sp.wait_ge(output_ready, n + 1)
                sp.dma_start(out_blocks[n], xT[:, n, :]).then_inc(banks_stored, 16)
            sp.wait_ge(late_stored, 16)
            sp.wait_ge(banks_stored, 16 * WIDTHS[-1])

        @block.gpsimd
        def _(pool):
            nc.gpsimd.memset(centering[:, :], -1.0 / P).then_inc(centering_zeroed, 1)
            nc.gpsimd.memset(mean_col[:, :], 1.0 / P).then_inc(constants_ready, 1)
            nc.gpsimd.memset(minus_half[:, :], -0.5).then_inc(constants_ready, 1)
            pool.wait_ge(centering_zeroed, 1)
            nc.gpsimd.affine_select(out=centering[:, :], in_=centering[:, :], compare_op=ALU.not_equal,
                                    fill=1.0 - 1.0 / P, base=0, pattern=[[-1, P]],
                                    channel_multiplier=1).then_inc(constants_ready, 1)
            pool.wait_ge(constants_ready, 3)

            def inverse_deviation(n):
                pool.wait_ge(var_ready, n + 1)
                if not (isinstance(n, int) and n == 0):
                    pool.wait_ge(support_ready, n)
                nc.gpsimd.tensor_tensor(rstd[:, :], var_eps[:, :], minus_half[:, :], ALU.pow)\
                    .then_inc(rstd_ready, 1)

            def weights(g, k, stage_b, stage_a):
                start = isinstance(k, int) and k == 0
                if g == 0:
                    pool.wait_ge(support_ready, k + 1)
                for r in range(UNROLL):
                    t = step_of(g, k, r)
                    if stage_b and r == 3:
                        inverse_deviation(k + 1)
                    if not (g == 0 and start):
                        pool.wait_ge(products_done, t - (WEIGHT_SLOTS - 1))
                    tile = support[:, bass.ds(k * UNROLL + r, 1), :]
                    nc.gpsimd.tensor_copy(sup_full[:, r:r + 1, :], tile).then_inc(sup_high_ready, 1)
                    nc.gpsimd.tensor_copy(sup_high[:, r:r + 1, :], tile).then_inc(sup_high_ready, 1)
                    pool.wait_ge(sup_high_ready, t * 2 + 2)
                    nc.gpsimd.tensor_tensor(sup_low[:, r, :], sup_full[:, r, :],
                                            sup_high[:, r, :].bitcast(F32), ALU.subtract)\
                        .then_inc(weights_ready, 1)
                if g == 1 and start:
                    early = slice(0, STORED_LATE[0])
                    pool.wait_ge(output_ready, STORED_LATE[0])
                    pool.dma_start(out_blocks[early].rearrange("n p c -> p n c"),
                                   xT[:, early, :]).then_inc(early_stored, 16)

            inverse_deviation(0)
            in_all_groups(pool, weights)
            pool.wait_ge(early_stored, 16)

        @block.scalar
        def _(act):
            def square(n):
                act.wait_ge(rectified_ready, n + 1)
                nc.scalar.activation(squares[:, :], centered_ps, ACT.Square).then_inc(squared, 1)

            def drain(n):
                if n >= 2:
                    act.wait_ge(output_ready, n - 1)
                nc.scalar.activation(relu_out[:, n % 2, :], banks[:, n % PSUM_BANKS, :], ACT.Relu,
                                     bias=bias[:, 0:1]).then_inc(bank_drained, 1)

            def round_high(g, k, stage_b, stage_a):
                start = isinstance(k, int) and k == 0
                width = WIDTHS[g] * BANK
                for r in range(UNROLL):
                    t = step_of(g, k, r)
                    if not is_last(g, k, r):
                        act.wait_ge(adj_landed[r], landed_count(g, k))
                    if not (g == 0 and start and r < SPLIT_SLOTS):
                        act.wait_ge(products_done, t - (SPLIT_SLOTS - 1))
                    if is_last(g, k, r):
                        for c in range(WIDTHS[g]):
                            cols = slice(c * BANK, (c + 1) * BANK)
                            act.wait_ge(piece_landed[c], 16)
                            nc.scalar.activation(adj_high[:, r % SPLIT_SLOTS, cols],
                                                 adj_tile[:, r, cols], ACT.Copy).then_inc(piece_high, 1)
                        continue
                    nc.scalar.activation(adj_high[:, r % SPLIT_SLOTS, 0:width], adj_tile[:, r, 0:width],
                                         ACT.Copy).then_inc(high_ready, 1)
                    if stage_a and r == 3:
                        square(k + 2)
                    for n in drained_after(g, k, r):
                        act.wait_ge(products_done, g * TILES)
                        drain(n)

            square(0)
            act.wait_ge(params_landed, 32)
            square(1)
            in_all_groups(act, round_high)
            for c in range(WIDTHS[-1]):
                act.wait_ge(piece_products, c + 1)
                drain(FIRST_BLOCK[-1] + c)

        @block.vector
        def _(dve):
            def rectify(n):
                dve.wait_ge(centered, n + 1)
                nc.vector.tensor_scalar(rectified[:, :], centered_ps, 0.0, None, ALU.max)\
                    .then_inc(rectified_ready, 1)

            def variance(n):
                dve.wait_ge(projected, n + 1)
                nc.vector.tensor_scalar(var_eps[:, :], var_ps, EPS, None, ALU.add).then_inc(var_ready, 1)

            def scale_support(n):
                dve.wait_ge(rstd_ready, n + 1)
                nc.vector.tensor_tensor(support[:, bass.ds(n * UNROLL, UNROLL), :],
                                        support_ps.rearrange("p (t d) -> p t d", d=P),
                                        rstd[:, :].rearrange("p (t o) -> p t o", o=1)
                                        .to_broadcast([P, UNROLL, P]), ALU.mult)\
                    .then_inc(support_ready, 1)

            def add_x(n):
                dve.wait_ge(bank_drained, n + 1)
                nc.vector.tensor_tensor(xT[:, n, :], xT[:, n, :], relu_out[:, n % 2, :], ALU.add)\
                    .then_inc(output_ready, 1)

            def round_low(g, k, stage_b, stage_a):
                width = WIDTHS[g] * BANK
                for r in range(UNROLL):
                    if is_last(g, k, r):
                        for c in range(WIDTHS[g]):
                            cols = slice(c * BANK, (c + 1) * BANK)
                            dve.wait_ge(piece_high, c + 1)
                            nc.vector.tensor_tensor(adj_low[:, r % SPLIT_SLOTS, cols],
                                                    adj_tile[:, r, cols],
                                                    adj_high[:, r % SPLIT_SLOTS, cols].bitcast(F32),
                                                    ALU.subtract).then_inc(piece_low, 1)
                        continue
                    dve.wait_ge(high_ready, step_of(g, k, r) + 1)
                    nc.vector.tensor_tensor(adj_low[:, r % SPLIT_SLOTS, 0:width], adj_tile[:, r, 0:width],
                                            adj_high[:, r % SPLIT_SLOTS, 0:width].bitcast(F32),
                                            ALU.subtract).then_inc(low_ready, 1)
                    if stage_b and r == 1:
                        variance(k + 1)
                    if stage_b and r == 2:
                        scale_support(k + 1)
                    if stage_a and r == 2:
                        rectify(k + 2)
                    for n in drained_after(g, k, r):
                        add_x(n)

            rectify(0)
            variance(0)
            scale_support(0)
            rectify(1)
            in_all_groups(dve, round_low)
            for n in range(FIRST_BLOCK[-1], COL_BLOCKS):
                add_x(n)

        @block.tensor
        def _(pe):
            def center(n):
                pe.wait_ge(x_landed, n * 16 + 16)
                if not (isinstance(n, int) and n == 0):
                    pe.wait_ge(var_ready, n)
                nc.tensor.matmul(banks[:, CENTER_BANK:CENTER_BANK + 1, :], centering[:, :],
                                 xT[:, bass.ds(n, 1), :], start=True, stop=True).then_inc(centered, 1)

            def project(n):
                pe.wait_ge(squared, n + 1)
                if not (isinstance(n, int) and n == 0):
                    pe.wait_ge(support_ready, n)
                for i in range(UNROLL):
                    nc.tensor.matmul(var_ps[:, i:i + 1], squares[:, i * P:(i + 1) * P], mean_col[:, :],
                                     start=True, stop=True)
                for i in range(UNROLL):
                    last = nc.tensor.matmul(support_ps[:, i * P:(i + 1) * P],
                                            rectified[:, i * P:(i + 1) * P], W_sb[:, :],
                                            start=True, stop=True)
                last.then_inc(projected, 1)

            def round_products(g, k, stage_b, stage_a):
                start, end = (isinstance(k, int) and k == edge for edge in (0, ROUNDS - 1))
                for r in range(UNROLL):
                    t = step_of(g, k, r)
                    opens, closes = start and r == 0, end and r == UNROLL - 1
                    if stage_a and r == 2:
                        center(k + 2)
                    pe.wait_ge(weights_ready, t + 1)
                    parts = [(sup_high, adj_high), (sup_low, adj_high), (sup_high, adj_low)]
                    if is_last(g, k, r):
                        for c in range(WIDTHS[g]):
                            for i, (sup, adj) in enumerate(parts):
                                if i == 0:
                                    pe.wait_ge(piece_high, c + 1)
                                if i == 2:
                                    pe.wait_ge(piece_low, c + 1)
                                last = nc.tensor.matmul(banks[:, (FIRST_BLOCK[g] + c) % PSUM_BANKS, :],
                                                        sup[:, r, :],
                                                        adj[:, r % SPLIT_SLOTS, c * BANK:(c + 1) * BANK],
                                                        start=False, stop=i == 2)
                            last.then_inc(piece_products, 1)
                        continue
                    pe.wait_ge(high_ready, t + 1)
                    for i, (sup, adj) in enumerate(parts):
                        if i == 2:
                            pe.wait_ge(low_ready, t + 1)
                        for c in range(WIDTHS[g]):
                            n = FIRST_BLOCK[g] + c
                            if opens and i == 0 and n >= PSUM_BANKS:
                                pe.wait_ge(bank_drained, n - PSUM_BANKS + 1)
                            last = nc.tensor.matmul(banks[:, n % PSUM_BANKS, :], sup[:, r, :],
                                                    adj[:, r % SPLIT_SLOTS, c * BANK:(c + 1) * BANK],
                                                    start=opens and i == 0, stop=closes and i == 2)
                    last.then_inc(products_done, 1)
                if stage_a:
                    project(k + 2)

            pe.wait_ge(constants_ready, 3)
            center(0)
            pe.wait_ge(params_landed, 32)
            project(0)
            center(1)
            project(1)
            in_all_groups(pe, round_products)


def kernel(x, adj, L0_gnn_W, L0_gnn_b):
    import numpy as np
    import concourse.bacc as bacc
    from concourse.bass_utils import run_bass_kernel_spmd

    nc = bacc.Bacc("TRN2", target_bir_lowering=False, num_devices=1)
    x, adj = np.asarray(x), np.asarray(adj)
    arrays = {
        "x_blocks": np.ascontiguousarray(x.T.reshape(P, COL_BLOCKS, BANK).transpose(1, 0, 2)),
        "W": np.ascontiguousarray(L0_gnn_W),
        "b": np.ascontiguousarray(L0_gnn_b).reshape(P, 1),
    }
    for g, (first, width) in enumerate(zip(FIRST_BLOCK, WIDTHS)):
        rows = adj[first * BANK:(first + width) * BANK]
        arrays[f"adj{g}"] = np.ascontiguousarray(rows.T).reshape(TILES, P, width * BANK)
    ap = {name: nc.dram_tensor(name, a.shape, F32, kind="ExternalInput").ap() for name, a in arrays.items()}
    out = nc.dram_tensor("out_blocks", (COL_BLOCKS, P, BANK), F32, kind="ExternalOutput").ap()
    gnn_layer(nc, ap["x_blocks"], [ap[f"adj{g}"] for g in range(len(WIDTHS))], ap["W"], ap["b"], out)
    result = run_bass_kernel_spmd(nc, [arrays], core_ids=[0]).results[0]["out_blocks"]
    return np.ascontiguousarray(result.transpose(0, 2, 1)).reshape(N, P)
```

```python
from contextlib import ExitStack

import concourse.bass as bass
from concourse import mybir

P = 128
BANK = 512
N = 8192
TILES = N // P
COL_BLOCKS = N // BANK
PSUM_BANKS = 8
UNROLL = BANK // P
ROUNDS = TILES // UNROLL
WIDTHS = [6, 5, 5]
FIRST_BLOCK = [0, 6, 11]
ADJ_SLOTS = UNROLL
SPLIT_SLOTS = 2
WEIGHT_SLOTS = UNROLL
DRAINED = [[0, 3, 1, 2], [0, 2, 1, 2]]
STORED_LATE = range(1, FIRST_BLOCK[-1])
RELU_SLOTS = 6
CENTER_BANK, SUPPORT_BANK = 6, 7
EPS = 1e-5

ALU = mybir.AluOpType
ACT = mybir.ActivationFunctionType
F32 = mybir.dt.float32
F32R = mybir.dt.float32r


def gnn_layer(nc, x_blocks, adj_groups, W, b, out_blocks):
    assert sum(WIDTHS) == COL_BLOCKS and ADJ_SLOTS == WEIGHT_SLOTS == UNROLL
    with ExitStack() as ctx:
        def sb(name, shape, dt=F32):
            return ctx.enter_context(nc.sbuf_tensor(name, shape, dt))

        def sem(name):
            return ctx.enter_context(nc.semaphore(name))

        widest = max(WIDTHS) * BANK
        xT = sb("xT", [P, COL_BLOCKS, BANK])
        support = sb("support", [P, TILES, P])
        adj_tile = sb("adj_tile", [P, ADJ_SLOTS, widest])
        adj_high = sb("adj_high", [P, SPLIT_SLOTS, widest], F32R)
        adj_low = sb("adj_low", [P, SPLIT_SLOTS, widest], F32R)
        sup_high = sb("sup_high", [P, WEIGHT_SLOTS, P], F32R)
        sup_low = sb("sup_low", [P, WEIGHT_SLOTS, P], F32R)
        W_sb = sb("W_sb", [P, P])
        bias = sb("bias", [P, 1])
        centering = sb("centering", [P, P])
        mean_col = sb("mean_col", [P, 1])
        minus_half = sb("minus_half", [P, UNROLL])
        squares = sb("squares", [P, BANK])
        rectified = sb("rectified", [P, BANK])
        var_eps = sb("var_eps", [P, UNROLL])
        rstd = sb("rstd", [P, UNROLL])
        relu_out = sb("relu_out", [P, RELU_SLOTS, BANK])
        banks = ctx.enter_context(nc.psum_tensor("banks", [P, PSUM_BANKS, BANK], F32))
        centered_ps = banks[:, CENTER_BANK, :]
        var_ps = banks[:, CENTER_BANK, 0:UNROLL]
        support_ps = banks[:, SUPPORT_BANK, :]

        adj_landed = [sem(f"adj_landed{s}") for s in range(ADJ_SLOTS)]
        piece_landed = [sem(f"piece_landed{c}") for c in range(WIDTHS[-1])]
        piece_high = sem("piece_high")
        piece_low = sem("piece_low")
        piece_products = sem("piece_products")
        x_landed = sem("x_landed")
        params_landed = sem("params_landed")
        centering_zeroed = sem("centering_zeroed")
        constants_ready = sem("constants_ready")
        high_ready = sem("high_ready")
        low_ready = sem("low_ready")
        sup_low_ready = sem("sup_low_ready")
        high_used = sem("high_used")
        products_done = sem("products_done")
        centered = sem("centered")
        squared = sem("squared")
        rectified_ready = sem("rectified_ready")
        projected = sem("projected")
        var_ready = sem("var_ready")
        rstd_ready = sem("rstd_ready")
        support_ready = sem("support_ready")
        bank_drained = sem("bank_drained")
        output_ready = sem("output_ready")
        early_stored = sem("early_stored")
        late_stored = sem("late_stored")
        banks_stored = sem("banks_stored")
        block = ctx.enter_context(nc.Block())

        def in_all_groups(eng, round_steps):
            round_steps(0, 0, True, True)
            with eng.Fori(1, ROUNDS - 2) as k:
                round_steps(0, k, True, True)
            round_steps(0, ROUNDS - 2, True, False)
            round_steps(0, ROUNDS - 1, False, False)
            for g in range(1, len(WIDTHS)):
                round_steps(g, 0, False, False)
                with eng.Fori(1, ROUNDS - 1) as k:
                    round_steps(g, k, False, False)
                round_steps(g, ROUNDS - 1, False, False)

        def step_of(g, k, r):
            return k * UNROLL + (g * TILES + r)

        def landed_count(g, k):
            return k * 16 + 16 * (g * ROUNDS + 1)

        def is_last(g, k, r):
            return g == len(WIDTHS) - 1 and isinstance(k, int) and k == ROUNDS - 1 and r == UNROLL - 1

        def drained_after(g, k, r):
            if g == 0 or not isinstance(k, int) or k > 0:
                return range(0)
            counts = DRAINED[g - 1]
            assert sum(counts) == WIDTHS[g - 1]
            first = FIRST_BLOCK[g - 1] + sum(counts[:r])
            return range(first, first + counts[r])

        @block.sync
        def _(sp):
            sp.dma_start(xT[:, 0, :], x_blocks[0]).then_inc(x_landed, 16)
            sp.dma_start(W_sb[:, :], W).then_inc(params_landed, 16)
            sp.dma_start(bias[:, :], b).then_inc(params_landed, 16)

            def load_x(n):
                sp.wait_ge(x_landed, n * 16)
                sp.dma_start(xT[:, bass.ds(n, 1), :], x_blocks[bass.ds(n, 1)].rearrange("o p c -> p o c"))\
                  .then_inc(x_landed, 16)

            def loads(g, k, stage_b, stage_a):
                width = WIDTHS[g] * BANK
                first = g == 0 and isinstance(k, int) and k == 0
                for r in range(UNROLL):
                    if first and r == 1:
                        load_x(1)
                    if g == 1 and r == 0 and isinstance(k, int) and k == ROUNDS - 1:
                        sp.wait_ge(output_ready, STORED_LATE[0])
                        early = slice(0, STORED_LATE[0])
                        sp.dma_start(out_blocks[early].rearrange("n p c -> p n c"), xT[:, early, :])\
                          .then_inc(early_stored, 16)
                    if r == 2 and stage_a:
                        load_x(k + 2)
                    if not first:
                        sp.wait_ge(low_ready, step_of(g, k, r) - (ADJ_SLOTS - 1))
                    if is_last(g, k, r):
                        for c in range(WIDTHS[g]):
                            cols = slice(c * BANK, (c + 1) * BANK)
                            sp.dma_start(adj_tile[:, r, cols], adj_groups[g][TILES - 1][:, cols])\
                              .then_inc(piece_landed[c], 16)
                        continue
                    sp.dma_start(adj_tile[:, r:r + 1, 0:width],
                                 adj_groups[g][bass.ds(k * UNROLL + r, 1)].rearrange("o p c -> p o c"))\
                      .then_inc(adj_landed[r], 16)

            in_all_groups(sp, loads)
            sp.wait_ge(output_ready, STORED_LATE[-1] + 1)
            late = slice(STORED_LATE[0], STORED_LATE[-1] + 1)
            sp.dma_start(out_blocks[late].rearrange("n p c -> p n c"), xT[:, late, :])\
              .then_inc(late_stored, 16)
            for n in range(FIRST_BLOCK[-1], COL_BLOCKS):
                sp.wait_ge(output_ready, n + 1)
                sp.dma_start(out_blocks[n], xT[:, n, :]).then_inc(banks_stored, 16)
            sp.wait_ge(early_stored, 16)
            sp.wait_ge(late_stored, 16)
            sp.wait_ge(banks_stored, 16 * WIDTHS[-1])

        @block.gpsimd
        def _(pool):
            nc.gpsimd.memset(centering[:, :], -1.0 / P).then_inc(centering_zeroed, 1)
            nc.gpsimd.memset(mean_col[:, :], 1.0 / P).then_inc(constants_ready, 1)
            nc.gpsimd.memset(minus_half[:, :], -0.5).then_inc(constants_ready, 1)
            pool.wait_ge(centering_zeroed, 1)
            nc.gpsimd.affine_select(out=centering[:, :], in_=centering[:, :], compare_op=ALU.not_equal,
                                    fill=1.0 - 1.0 / P, base=0, pattern=[[-1, P]],
                                    channel_multiplier=1).then_inc(constants_ready, 1)
            pool.wait_ge(constants_ready, 3)

            def inverse_deviation(n):
                pool.wait_ge(var_ready, n + 1)
                if not (isinstance(n, int) and n == 0):
                    pool.wait_ge(support_ready, n)
                nc.gpsimd.tensor_tensor(rstd[:, :], var_eps[:, :], minus_half[:, :], ALU.pow)\
                    .then_inc(rstd_ready, 1)

            inverse_deviation(0)
            with pool.Fori(1, ROUNDS) as n:
                inverse_deviation(n)

        @block.scalar
        def _(act):
            def square(n):
                act.wait_ge(rectified_ready, n + 1)
                nc.scalar.activation(squares[:, :], centered_ps, ACT.Square).then_inc(squared, 1)

            def drain(n):
                if n >= RELU_SLOTS:
                    act.wait_ge(output_ready, n - (RELU_SLOTS - 1))
                nc.scalar.activation(relu_out[:, n % RELU_SLOTS, :], banks[:, n % PSUM_BANKS, :], ACT.Relu,
                                     bias=bias[:, 0:1]).then_inc(bank_drained, 1)

            def round_high(g, k, stage_b, stage_a):
                start = isinstance(k, int) and k == 0
                width = WIDTHS[g] * BANK
                if g == 0:
                    act.wait_ge(support_ready, k + 1)
                for r in range(UNROLL):
                    t = step_of(g, k, r)
                    nc.scalar.activation(sup_high[:, r:r + 1, :],
                                         support[:, bass.ds(k * UNROLL + r, 1), :],
                                         ACT.Copy).then_inc(high_ready, 1)
                    if not (g == 0 and start and r < SPLIT_SLOTS):
                        act.wait_ge(low_ready, t - (SPLIT_SLOTS - 1))
                        act.wait_ge(high_used, t - (SPLIT_SLOTS - 1))
                    if not is_last(g, k, r):
                        act.wait_ge(adj_landed[r], landed_count(g, k))
                    if is_last(g, k, r):
                        for c in range(WIDTHS[g]):
                            cols = slice(c * BANK, (c + 1) * BANK)
                            act.wait_ge(piece_landed[c], 16)
                            nc.scalar.activation(adj_high[:, r % SPLIT_SLOTS, cols],
                                                 adj_tile[:, r, cols], ACT.Copy).then_inc(piece_high, 1)
                        continue
                    nc.scalar.activation(adj_high[:, r % SPLIT_SLOTS, 0:width], adj_tile[:, r, 0:width],
                                         ACT.Copy).then_inc(high_ready, 1)
                    if stage_a and r == 3:
                        square(k + 2)
                    for n in drained_after(g, k, r):
                        act.wait_ge(products_done, g * TILES)
                        drain(n)

            square(0)
            act.wait_ge(params_landed, 32)
            square(1)
            in_all_groups(act, round_high)
            for c in range(WIDTHS[-1]):
                act.wait_ge(piece_products, c + 1)
                drain(FIRST_BLOCK[-1] + c)

        @block.vector
        def _(dve):
            def rectify(n):
                dve.wait_ge(centered, n + 1)
                nc.vector.tensor_scalar(rectified[:, :], centered_ps, 0.0, None, ALU.max)\
                    .then_inc(rectified_ready, 1)

            def variance(n):
                dve.wait_ge(projected, n + 1)
                nc.vector.tensor_scalar(var_eps[:, :], var_ps, EPS, None, ALU.add).then_inc(var_ready, 1)

            def scale_support(n):
                dve.wait_ge(rstd_ready, n + 1)
                nc.vector.tensor_tensor(support[:, bass.ds(n * UNROLL, UNROLL), :],
                                        support_ps.rearrange("p (t d) -> p t d", d=P),
                                        rstd[:, :].rearrange("p (t o) -> p t o", o=1)
                                        .to_broadcast([P, UNROLL, P]), ALU.mult)\
                    .then_inc(support_ready, 1)

            def add_x(n):
                dve.wait_ge(bank_drained, n + 1)
                nc.vector.tensor_tensor(xT[:, n, :], xT[:, n, :], relu_out[:, n % RELU_SLOTS, :], ALU.add)\
                    .then_inc(output_ready, 1)

            def round_low(g, k, stage_b, stage_a):
                start = isinstance(k, int) and k == 0
                width = WIDTHS[g] * BANK
                for r in range(UNROLL):
                    t = step_of(g, k, r)
                    dve.wait_ge(high_ready, t * 2 + 1)
                    nc.vector.tensor_tensor(sup_low[:, r:r + 1, :],
                                            support[:, bass.ds(k * UNROLL + r, 1), :],
                                            sup_high[:, r:r + 1, :].bitcast(F32),
                                            ALU.subtract).then_inc(sup_low_ready, 1)
                    if not (g == 0 and start and r < SPLIT_SLOTS):
                        dve.wait_ge(products_done, t - (SPLIT_SLOTS - 1))
                    if is_last(g, k, r):
                        for c in range(WIDTHS[g]):
                            cols = slice(c * BANK, (c + 1) * BANK)
                            dve.wait_ge(piece_high, c + 1)
                            nc.vector.tensor_tensor(adj_low[:, r % SPLIT_SLOTS, cols],
                                                    adj_tile[:, r, cols],
                                                    adj_high[:, r % SPLIT_SLOTS, cols].bitcast(F32),
                                                    ALU.subtract).then_inc(piece_low, 1)
                        continue
                    dve.wait_ge(high_ready, t * 2 + 2)
                    nc.vector.tensor_tensor(adj_low[:, r % SPLIT_SLOTS, 0:width], adj_tile[:, r, 0:width],
                                            adj_high[:, r % SPLIT_SLOTS, 0:width].bitcast(F32),
                                            ALU.subtract).then_inc(low_ready, 1)
                    if stage_b and r == 1:
                        variance(k + 1)
                    if stage_b and r == 2:
                        scale_support(k + 1)
                    if stage_a and r == 2:
                        rectify(k + 2)
                    for n in drained_after(g, k, r):
                        add_x(n)

            rectify(0)
            variance(0)
            scale_support(0)
            rectify(1)
            in_all_groups(dve, round_low)
            for n in range(FIRST_BLOCK[-1], COL_BLOCKS):
                add_x(n)

        @block.tensor
        def _(pe):
            def center(n):
                pe.wait_ge(x_landed, n * 16 + 16)
                if not (isinstance(n, int) and n == 0):
                    pe.wait_ge(var_ready, n)
                nc.tensor.matmul(banks[:, CENTER_BANK:CENTER_BANK + 1, :], centering[:, :],
                                 xT[:, bass.ds(n, 1), :], start=True, stop=True).then_inc(centered, 1)

            def project(n):
                pe.wait_ge(squared, n + 1)
                if not (isinstance(n, int) and n == 0):
                    pe.wait_ge(support_ready, n)
                for i in range(UNROLL):
                    nc.tensor.matmul(var_ps[:, i:i + 1], squares[:, i * P:(i + 1) * P], mean_col[:, :],
                                     start=True, stop=True)
                for i in range(UNROLL):
                    last = nc.tensor.matmul(support_ps[:, i * P:(i + 1) * P],
                                            rectified[:, i * P:(i + 1) * P], W_sb[:, :],
                                            start=True, stop=True)
                last.then_inc(projected, 1)

            def round_products(g, k, stage_b, stage_a):
                start, end = (isinstance(k, int) and k == edge for edge in (0, ROUNDS - 1))
                for r in range(UNROLL):
                    t = step_of(g, k, r)
                    opens, closes = start and r == 0, end and r == UNROLL - 1
                    if stage_a and r == 2:
                        center(k + 2)
                    parts = [(sup_high, adj_high), (sup_low, adj_high), (sup_high, adj_low)]
                    if is_last(g, k, r):
                        for c in range(WIDTHS[g]):
                            for i, (sup, adj) in enumerate(parts):
                                if i == 0:
                                    pe.wait_ge(piece_high, c + 1)
                                if i == 1 and c == 0:
                                    pe.wait_ge(sup_low_ready, t + 1)
                                if i == 2:
                                    pe.wait_ge(piece_low, c + 1)
                                last = nc.tensor.matmul(banks[:, (FIRST_BLOCK[g] + c) % PSUM_BANKS, :],
                                                        sup[:, r, :],
                                                        adj[:, r % SPLIT_SLOTS, c * BANK:(c + 1) * BANK],
                                                        start=False, stop=i == 2)
                            last.then_inc(piece_products, 1)
                        continue
                    pe.wait_ge(high_ready, t * 2 + 2)
                    if opens:
                        pe.wait_ge(sup_low_ready, t + 1)
                        order = [(i, c) for c in range(WIDTHS[g]) for i in (0, 1)]
                    else:
                        order = [(i, c) for i in (0, 1) for c in range(WIDTHS[g])]
                    for i, c in order:
                        n = FIRST_BLOCK[g] + c
                        if opens and i == 0 and n >= PSUM_BANKS:
                            pe.wait_ge(bank_drained, n - PSUM_BANKS + 1)
                        if not opens and (i, c) == (1, 0):
                            pe.wait_ge(sup_low_ready, t + 1)
                        sup, adj = parts[i]
                        last = nc.tensor.matmul(banks[:, n % PSUM_BANKS, :], sup[:, r, :],
                                                adj[:, r % SPLIT_SLOTS, c * BANK:(c + 1) * BANK],
                                                start=opens and i == 0, stop=False)
                    last.then_inc(high_used, 1)
                    pe.wait_ge(low_ready, t + 1)
                    sup, adj = parts[2]
                    for c in range(WIDTHS[g]):
                        last = nc.tensor.matmul(banks[:, (FIRST_BLOCK[g] + c) % PSUM_BANKS, :], sup[:, r, :],
                                                adj[:, r % SPLIT_SLOTS, c * BANK:(c + 1) * BANK],
                                                start=False, stop=closes)
                    last.then_inc(products_done, 1)
                if stage_a:
                    project(k + 2)

            pe.wait_ge(constants_ready, 3)
            center(0)
            pe.wait_ge(params_landed, 32)
            project(0)
            center(1)
            project(1)
            in_all_groups(pe, round_products)


def kernel(x, adj, L0_gnn_W, L0_gnn_b):
    import numpy as np
    import concourse.bacc as bacc
    from concourse.bass_utils import run_bass_kernel_spmd

    nc = bacc.Bacc("TRN2", target_bir_lowering=False, num_devices=1)
    x, adj = np.asarray(x), np.asarray(adj)
    arrays = {
        "x_blocks": np.ascontiguousarray(x.T.reshape(P, COL_BLOCKS, BANK).transpose(1, 0, 2)),
        "W": np.ascontiguousarray(L0_gnn_W),
        "b": np.ascontiguousarray(L0_gnn_b).reshape(P, 1),
    }
    for g, (first, width) in enumerate(zip(FIRST_BLOCK, WIDTHS)):
        rows = adj[first * BANK:(first + width) * BANK]
        arrays[f"adj{g}"] = np.ascontiguousarray(rows.T).reshape(TILES, P, width * BANK)
    ap = {name: nc.dram_tensor(name, a.shape, F32, kind="ExternalInput").ap() for name, a in arrays.items()}
    out = nc.dram_tensor("out_blocks", (COL_BLOCKS, P, BANK), F32, kind="ExternalOutput").ap()
    gnn_layer(nc, ap["x_blocks"], [ap[f"adj{g}"] for g in range(len(WIDTHS))], ap["W"], ap["b"], out)
    result = run_bass_kernel_spmd(nc, [arrays], core_ids=[0]).results[0]["out_blocks"]
    return np.ascontiguousarray(result.transpose(0, 2, 1)).reshape(N, P)
```
